# Optimizing a Trainium2 kernel written in Bass

```python
import numpy as np
import jax
import jax.numpy as jnp

def _softmax(x, axis=-1):
    return jax.nn.softmax(x, axis=axis)

def _gelu(x):
    return jax.nn.gelu(x, approximate=True)

def _silu(x):
    return jax.nn.silu(x)

def _sigmoid(x):
    return jax.nn.sigmoid(x)

def _layernorm(x, axis=-1, eps=1e-05):
    m = jnp.mean(x, axis=axis, keepdims=True)
    v = jnp.var(x, axis=axis, keepdims=True)
    return (x - m) / jnp.sqrt(v + eps)

def _scatter_add(tgt, idx, src, axis=0):
    return tgt.at[idx].add(src)

def _segment_sum(src, seg, n):
    return jax.ops.segment_sum(src, seg, n)
kernel_name = 'mk_dlrm_tower_d1_rec_r8_a82f13'

def setup_inputs(seed: int=0):
    np.random.seed(seed)
    _w = jnp.asarray

    def _rec_inputs():
        import jax
        import jax.numpy as jnp
        _tk = jax.random.key(seed)
        ids = jnp.stack([jax.random.randint(jax.random.fold_in(_tk, 200 + f), (512,), 0, v, jnp.int32) for f, v in enumerate([1250, 12500, 125000, 1000, 12500, 1000, 1000, 1250, 12500, 1250, 1000, 1000, 1000, 1000, 12500, 1250, 1000, 12500, 12500, 12500, 1000, 1000, 1000, 12500, 1250, 1000])], axis=1)
        tbl_0 = 0.05 * jax.random.normal(jax.random.fold_in(_tk, 500 + 0), (1250, 128), jnp.float32)
        tbl_1 = 0.05 * jax.random.normal(jax.random.fold_in(_tk, 500 + 1), (12500, 128), jnp.float32)
        tbl_2 = 0.05 * jax.random.normal(jax.random.fold_in(_tk, 500 + 2), (125000, 128), jnp.float32)
        tbl_3 = 0.05 * jax.random.normal(jax.random.fold_in(_tk, 500 + 3), (1000, 128), jnp.float32)
        tbl_4 = 0.05 * jax.random.normal(jax.random.fold_in(_tk, 500 + 4), (12500, 128), jnp.float32)
        tbl_5 = 0.05 * jax.random.normal(jax.random.fold_in(_tk, 500 + 5), (1000, 128), jnp.float32)
        tbl_6 = 0.05 * jax.random.normal(jax.random.fold_in(_tk, 500 + 6), (1000, 128), jnp.float32)
        tbl_7 = 0.05 * jax.random.normal(jax.random.fold_in(_tk, 500 + 7), (1250, 128), jnp.float32)
        tbl_8 = 0.05 * jax.random.normal(jax.random.fold_in(_tk, 500 + 8), (12500, 128), jnp.float32)
        tbl_9 = 0.05 * jax.random.normal(jax.random.fold_in(_tk, 500 + 9), (1250, 128), jnp.float32)
        tbl_10 = 0.05 * jax.random.normal(jax.random.fold_in(_tk, 500 + 10), (1000, 128), jnp.float32)
        tbl_11 = 0.05 * jax.random.normal(jax.random.fold_in(_tk, 500 + 11), (1000, 128), jnp.float32)
        tbl_12 = 0.05 * jax.random.normal(jax.random.fold_in(_tk, 500 + 12), (1000, 128), jnp.float32)
        tbl_13 = 0.05 * jax.random.normal(jax.random.fold_in(_tk, 500 + 13), (1000, 128), jnp.float32)
        tbl_14 = 0.05 * jax.random.normal(jax.random.fold_in(_tk, 500 + 14), (12500, 128), jnp.float32)
        tbl_15 = 0.05 * jax.random.normal(jax.random.fold_in(_tk, 500 + 15), (1250, 128), jnp.float32)
        tbl_16 = 0.05 * jax.random.normal(jax.random.fold_in(_tk, 500 + 16), (1000, 128), jnp.float32)
        tbl_17 = 0.05 * jax.random.normal(jax.random.fold_in(_tk, 500 + 17), (12500, 128), jnp.float32)
        tbl_18 = 0.05 * jax.random.normal(jax.random.fold_in(_tk, 500 + 18), (12500, 128), jnp.float32)
        tbl_19 = 0.05 * jax.random.normal(jax.random.fold_in(_tk, 500 + 19), (12500, 128), jnp.float32)
        tbl_20 = 0.05 * jax.random.normal(jax.random.fold_in(_tk, 500 + 20), (1000, 128), jnp.float32)
        tbl_21 = 0.05 * jax.random.normal(jax.random.fold_in(_tk, 500 + 21), (1000, 128), jnp.float32)
        tbl_22 = 0.05 * jax.random.normal(jax.random.fold_in(_tk, 500 + 22), (1000, 128), jnp.float32)
        tbl_23 = 0.05 * jax.random.normal(jax.random.fold_in(_tk, 500 + 23), (12500, 128), jnp.float32)
        tbl_24 = 0.05 * jax.random.normal(jax.random.fold_in(_tk, 500 + 24), (1250, 128), jnp.float32)
        tbl_25 = 0.05 * jax.random.normal(jax.random.fold_in(_tk, 500 + 25), (1000, 128), jnp.float32)
        _rk = jax.random.fold_in(_tk, 7)
        r_dense_features = -0.000520686 + 1.00062 * jax.random.normal(jax.random.fold_in(_rk, 101), (512, 128), jnp.float32)
        W_top1 = 0.0405887 * jax.random.normal(jax.random.fold_in(_tk, 801), (607, 512), jnp.float32)
        W_top2 = 0.0441942 * jax.random.normal(jax.random.fold_in(_tk, 802), (512, 256), jnp.float32)
        W_top3 = 0.0625 * jax.random.normal(jax.random.fold_in(_tk, 803), (256, 1), jnp.float32)
        b_top1 = jnp.zeros((512,), jnp.float32)
        b_top2 = jnp.zeros((256,), jnp.float32)
        return (r_dense_features, ids, tbl_0, tbl_1, tbl_2, tbl_3, tbl_4, tbl_5, tbl_6, tbl_7, tbl_8, tbl_9, tbl_10, tbl_11, tbl_12, tbl_13, tbl_14, tbl_15, tbl_16, tbl_17, tbl_18, tbl_19, tbl_20, tbl_21, tbl_22, tbl_23, tbl_24, tbl_25, W_top1, b_top1, W_top2, b_top2, W_top3)
    r_dense_features, ids, tbl_0, tbl_1, tbl_2, tbl_3, tbl_4, tbl_5, tbl_6, tbl_7, tbl_8, tbl_9, tbl_10, tbl_11, tbl_12, tbl_13, tbl_14, tbl_15, tbl_16, tbl_17, tbl_18, tbl_19, tbl_20, tbl_21, tbl_22, tbl_23, tbl_24, tbl_25, W_top1, b_top1, W_top2, b_top2, W_top3 = _rec_inputs()

    def _L0_rec_setup():
        import jax, jax.numpy as jnp
        import numpy as np
        NUM_SPARSE = 26
        EMBED_DIM = 128
        BATCH = 2048
        key = jax.random.key(seed)
        k1, k2 = jax.random.split(key)
        dense_features = jax.random.normal(k1, (BATCH, EMBED_DIM), dtype=jnp.float32)
        sparse_features = jax.random.normal(k2, (BATCH, NUM_SPARSE, EMBED_DIM), dtype=jnp.float32)
        return {'dense_features': dense_features, 'sparse_features': sparse_features}
    _L0_rec_all = _L0_rec_setup()
    _L0_rec_in = {k: v for k, v in _L0_rec_all.items() if k in ()}
    del _L0_rec_all
    return {'r_dense_features': r_dense_features, 'ids': ids, 'tbl_0': tbl_0, 'tbl_1': tbl_1, 'tbl_2': tbl_2, 'tbl_3': tbl_3, 'tbl_4': tbl_4, 'tbl_5': tbl_5, 'tbl_6': tbl_6, 'tbl_7': tbl_7, 'tbl_8': tbl_8, 'tbl_9': tbl_9, 'tbl_10': tbl_10, 'tbl_11': tbl_11, 'tbl_12': tbl_12, 'tbl_13': tbl_13, 'tbl_14': tbl_14, 'tbl_15': tbl_15, 'tbl_16': tbl_16, 'tbl_17': tbl_17, 'tbl_18': tbl_18, 'tbl_19': tbl_19, 'tbl_20': tbl_20, 'tbl_21': tbl_21, 'tbl_22': tbl_22, 'tbl_23': tbl_23, 'tbl_24': tbl_24, 'tbl_25': tbl_25, 'W_top1': W_top1, 'b_top1': b_top1, 'W_top2': W_top2, 'b_top2': b_top2, 'W_top3': W_top3}

def reference(r_dense_features, ids, tbl_0, tbl_1, tbl_2, tbl_3, tbl_4, tbl_5, tbl_6, tbl_7, tbl_8, tbl_9, tbl_10, tbl_11, tbl_12, tbl_13, tbl_14, tbl_15, tbl_16, tbl_17, tbl_18, tbl_19, tbl_20, tbl_21, tbl_22, tbl_23, tbl_24, tbl_25, W_top1, b_top1, W_top2, b_top2, W_top3):
    import jax
    import jax.numpy as jnp

    def _L0_rec_ref(dense_features, sparse_features):
        import jax, jax.numpy as jnp
        import numpy as np
        NUM_SPARSE = 26
        EMBED_DIM = 128
        BATCH = 2048
        F = NUM_SPARSE + 1
        combined = jnp.concatenate([dense_features[:, None, :], sparse_features], axis=1)
        interactions = jnp.einsum('bfd,bgd->bfg', combined, combined)
        iu, ju = jnp.triu_indices(F, k=1)
        interactions_flat = interactions[:, iu, ju]
        return jnp.concatenate([dense_features, interactions_flat], axis=1)
    e = jnp.stack([tbl_0[ids[:, 0]], tbl_1[ids[:, 1]], tbl_2[ids[:, 2]], tbl_3[ids[:, 3]], tbl_4[ids[:, 4]], tbl_5[ids[:, 5]], tbl_6[ids[:, 6]], tbl_7[ids[:, 7]], tbl_8[ids[:, 8]], tbl_9[ids[:, 9]], tbl_10[ids[:, 10]], tbl_11[ids[:, 11]], tbl_12[ids[:, 12]], tbl_13[ids[:, 13]], tbl_14[ids[:, 14]], tbl_15[ids[:, 15]], tbl_16[ids[:, 16]], tbl_17[ids[:, 17]], tbl_18[ids[:, 18]], tbl_19[ids[:, 19]], tbl_20[ids[:, 20]], tbl_21[ids[:, 21]], tbl_22[ids[:, 22]], tbl_23[ids[:, 23]], tbl_24[ids[:, 24]], tbl_25[ids[:, 25]]], axis=1)
    z = _L0_rec_ref(r_dense_features, e)
    z = z.reshape(z.shape[0], -1)
    h = jnp.concatenate([z, r_dense_features], axis=1)
    h = jnp.maximum(h @ W_top1 + b_top1, 0.0)
    h = jnp.maximum(h @ W_top2 + b_top2, 0.0)
    y = h @ W_top3
    return y

_drawn_inputs = setup_inputs


def setup_inputs(seed=0):
    import zlib

    import numpy as np

    out = dict(_drawn_inputs(seed))
    spreads = {'b_top1': (0.0, 0.1), 'b_top2': (0.0, 0.1)}
    factors = {}
    for name, (base, spread) in spreads.items():
        noise = np.random.default_rng([zlib.crc32(name.encode()), seed]).standard_normal(out[name].shape)
        drawn = base * np.exp(spread * noise) if base else spread * noise
        out[name] = jnp.asarray(drawn.astype(out[name].dtype))
    for name, factor in factors.items():
        out[name] = (out[name] * factor).astype(out[name].dtype)
    return out
```

```python
from contextlib import ExitStack

import concourse.bass as bass
from concourse import mybir

B, D, NS = 512, 128, 26
P = 128
NF = NS + 1
NT = B // P
SLOTS = 32
NPAIR = NF * (NF - 1) // 2
H1, H2 = 512, 256
UH = H1 // P // 2
HOT = (3, 5, 6, 10, 11, 12, 13, 20)
NH = len(HOT)
COLD = tuple(f for f in range(NS) if f not in HOT)
HROWS, HC = 125, 8
NG = P // 4
GB = NG // 2
PB = 4
PER_LOOKUP_SEM = 4

TILE_SLOTS = (0,) + tuple(f + 1 for f in COLD)
USES = [TILE_SLOTS[i:i + PB] for i in range(0, len(TILE_SLOTS), PB)]
NU = len(USES)
KT = (NPAIR + P - 1) // P
KW = [min(P, NPAIR - k * P) for k in range(KT)]
PAIR0 = [a * (NF - 1) - a * (a - 1) // 2 for a in range(NF)]
CU = (NF - 1 + PB - 1) // PB
TAB_RING, OH_RING = 3, 6
assert NH % 2 == 0


def runs(slots):
    out = []
    for i, s in enumerate(slots):
        if out and out[-1][0] + out[-1][1] == s:
            out[-1][1] += 1
        else:
            out.append([s, 1, i])
    return out


def build(nc, dense, ids, idsT, tables, W1, b1, W2, b2, W3, out):
    fp32, fp32r, i32 = mybir.dt.float32, mybir.dt.float32r, mybir.dt.int32
    ALU, ACT = mybir.AluOpType, mybir.ActivationFunctionType

    with ExitStack() as ctx:
        def sb(name, shape, dt=fp32):
            return ctx.enter_context(nc.sbuf_tensor(name, shape, dt))

        def bank(name):
            return ctx.enter_context(nc.psum_tensor(name, [P, 512], fp32))

        def sem(name):
            return ctx.enter_context(nc.semaphore(name))

        ident = sb("ident", [P, P])
        row_of = sb("row_of", [HROWS, HC])
        idx = sb("idx", [P, NT, NS], i32)
        idb = sb("idb", [HROWS, NH, B], i32)
        rows = sb("rows", [P, NT, len(COLD), D])
        dn = sb("dn", [P, NT, D])
        tab = sb("tab", [HROWS, TAB_RING, HC * D])
        tab_hi = sb("tab_hi", [HROWS, 2, HC * D], fp32r)
        tab_lo = sb("tab_lo", [HROWS, 2, HC * D], fp32r)
        onehot = sb("onehot", [HROWS, OH_RING, B], fp32r)
        xT = sb("xT", [P, NT, P, SLOTS])
        dT = sb("dT", [P, NT, P])
        gram = sb("gram", [P, NF - 1, NG])
        zs = sb("zs", [NG, 4, NPAIR])
        zT = sb("zT", [P, KT, P])
        w1d = sb("w1d", [P, 2, H1])
        w1s = sb("w1s", [P, H1])
        w1z = sb("w1z", [P, KT, H1])
        w2 = sb("w2", [P, H1 // P, H2])
        w3 = sb("w3", [P, H2 // P])
        bias1 = sb("bias1", [P, H1 // P])
        bias2 = sb("bias2", [P, H2 // P])
        h1 = sb("h1", [P, H1 // P, P])
        h2 = sb("h2", [P, H2 // P, P])
        y = sb("y", [1, B])

        pA = [bank("pA0"), bank("pA1")]
        pG = [bank("pG0"), bank("pG1")]
        pC = [bank("pC0"), bank("pC1")]
        pZ = bank("pZ")
        pH = bank("pH")
        pL1 = [pH, pG[0]]
        pL2 = [pG[1], pZ]
        pY = pH

        s_idx, s_dn, s_wgt = sem("s_idx"), sem("s_dn"), sem("s_wgt")
        s_idb = [sem(f"s_idb{k}") for k in range(NH)]
        s_tab = [sem(f"s_tab{k}") for k in range(NH)]
        NL = (len(COLD) + PER_LOOKUP_SEM - 1) // PER_LOOKUP_SEM
        s_rows = [[sem(f"s_rows{t}_{n}") for n in range(NL)] for t in range(NT)]
        s_const = sem("s_const")
        s_pad = sem("s_pad")
        s_w1s = sem("s_w1s")
        s_hi, s_lo = sem("s_hi"), sem("s_lo")
        s_oh = sem("s_oh")
        s_oh_used = sem("s_oh_used")
        a_full = [sem("a_full0"), sem("a_full1")]
        a_free = [sem("a_free0"), sem("a_free1")]
        g_full = [sem("g_full0"), sem("g_full1")]
        g_free = [sem("g_free0"), sem("g_free1")]
        c_full = [sem("c_full0"), sem("c_full1")]
        c_free = [sem("c_free0"), sem("c_free1")]
        s_z, s_zT = sem("s_z"), sem("s_zT")
        l1_full, l1_free = [sem("l1_full0"), sem("l1_full1")], [sem("l1_free0"), sem("l1_free1")]
        l2_full, l2_free = [sem("l2_full0"), sem("l2_full1")], [sem("l2_free0"), sem("l2_free1")]
        s_y, s_yr = sem("s_y"), sem("s_yr")
        s_out = sem("s_out")

        def c_uses(t, j):
            return len([n for n in range(CU) if n % 2 == j]) * t

        def evacuate_features(eng, copy, j, t, n):
            v = t * NU + n
            eng.wait_ge(a_full[j], v // 2 + 1)
            if v % NU == 0:
                copy(dT[:, t, :], pA[j][:, 0:P])
            for first, count, at in runs(USES[n]):
                last = copy(xT[:, t, :, first:first + count].rearrange("p c f -> p f c"),
                            pA[j][:, at * P:(at + count) * P].rearrange("p (f c) -> p f c", f=count))
            last.then_inc(a_free[j], 1)

        def evacuate_hot(eng, copy, j, k):
            eng.wait_ge(s_oh_used, HC * (k + 1))
            copy(xT[:, :, :, HOT[k] + 1].rearrange("p t c -> p (t c)"), pA[j][:, :]).then_inc(a_free[j], 1)

        def evacuate_gram(eng, copy, j, t):
            eng.wait_ge(g_full[j], t + 1)
            if t:
                for i in range(2):
                    eng.wait_ge(c_full[i], c_uses(t, i))
            copy(gram[:, :, j * GB:(j + 1) * GB],
                 pG[j][:, 0:GB * (NF - 1)].rearrange("p (g a) -> p a g", g=GB)).then_inc(g_free[j], 1)

        def evacuate_pairs(eng, copy, j, t):
            if t:
                eng.wait_ge(s_z, t)
            for n in range(j, CU, 2):
                eng.wait_ge(c_full[j], c_uses(t, j) + n // 2 + 1)
                for a in range(n * PB, min((n + 1) * PB, NF - 1)):
                    src = pC[j][0:NG, (a % PB) * P:(a % PB + 1) * P].rearrange("g (q b) -> g q b", q=4)
                    last = copy(zs[:, :, PAIR0[a]:PAIR0[a + 1]], src[:, :, a + 1:NF])
                last.then_inc(c_free[j], 1)

        def evacuate_layer1(eng, relu, j, t):
            eng.wait_ge(l1_full[j], t + 1)
            if t:
                eng.wait_ge(l2_full[1], t)
            for i in range(UH):
                n = j * UH + i
                last = relu(h1[:, n, :], pL1[j][:, i * P:(i + 1) * P], bias1[:, n:n + 1])
            last.then_inc(l1_free[j], 1)

        def evacuate_layer2(eng, relu, j, t):
            eng.wait_ge(l2_full[j], t + 1)
            if t:
                eng.wait_ge(s_y, t)
            relu(h2[:, j, :], pL2[j][:, 0:P], bias2[:, j:j + 1]).then_inc(l2_free[j], 1)

        block = ctx.enter_context(nc.Block())

        @block.sync
        def _(sp):
            def load_table(k):
                if k >= TAB_RING:
                    sp.wait_ge(s_lo, k - TAB_RING + 1)
                sp.dma_start(tab[:, k % TAB_RING, :],
                             tables[HOT[k]].rearrange("(p c) d -> p (c d)", c=HC)).then_inc(s_tab[k], 16)

            sp.dma_start(idx[:, :, :], ids.rearrange("(t c) f -> c t f", t=NT)).then_inc(s_idx, 16)
            for k in range(NH):
                if k < TAB_RING:
                    load_table(k)
                sp.dma_start(idb[:, k, :], idsT[HOT[k], :].partition_broadcast(HROWS)).then_inc(s_idb[k], 16)
            sp.dma_start(dn[:, :, :], dense.rearrange("(t c) d -> c t d", t=NT)).then_inc(s_dn, 16)
            for i in range(2):
                r = i * (D + NPAIR)
                sp.dma_start(w1d[:, i, :], W1[r:r + D, :]).then_inc(s_wgt, 16)
            for k in range(KT):
                r = D + k * P
                sp.dma_start(w1z[0:KW[k], k, :], W1[r:r + KW[k], :]).then_inc(s_wgt, 16)
            sp.dma_start(w2[:, :, :], W2.rearrange("(n p) m -> p n m", p=P)).then_inc(s_wgt, 16)
            with nc.allow_non_contiguous_dma(reason="three vectors of a few hundred numbers"):
                sp.dma_start(w3[:, :], W3.rearrange("(n p) o -> p (n o)", p=P)).then_inc(s_wgt, 16)
                sp.dma_start(bias1[:, :], b1.rearrange("(n p) -> p n", p=P)).then_inc(s_wgt, 16)
                sp.dma_start(bias2[:, :], b2.rearrange("(n p) -> p n", p=P)).then_inc(s_wgt, 16)
            for k in range(TAB_RING, NH):
                load_table(k)
            sp.wait_ge(s_yr, NT)
            sp.dma_start(out.rearrange("(a n) o -> a (n o)", a=1), y[:, :]).then_inc(s_out, 16)
            sp.wait_ge(s_out, 16)

        WEIGHTS = 16 * (2 + KT + 4)

        @block.gpsimd
        def _(pool):
            nc.gpsimd.iota(row_of[:, :], [[1, HC]], base=0, channel_multiplier=HC,
                           allow_small_or_imprecise_dtypes=True).then_inc(s_const, 1)
            nc.gpsimd.memset(ident[:, :], 0.0).then_inc(s_const, 1)
            pool.wait_ge(s_const, 2)
            nc.gpsimd.affine_select(out=ident[:, :], in_=ident[:, :], compare_op=ALU.not_equal, fill=1.0,
                                    base=0, pattern=[[-1, P]], channel_multiplier=1).then_inc(s_const, 1)
            pool.wait_ge(s_idx, 16)
            for t in range(NT):
                for i, f in enumerate(COLD):
                    pool.indirect_dma_start(rows[:, t, i, :], None, tables[f],
                                            bass.IndirectOffsetOnAxis(ap=idx[:, t, f:f + 1], axis=0)
                                            ).then_inc(s_rows[t][i // PER_LOOKUP_SEM], 16)

        @block.scalar
        def _(act):
            copy = nc.scalar.copy

            def relu(dst, src, bias):
                return nc.scalar.activation(dst, src, ACT.Relu, bias=bias)

            def hot(k):
                act.wait_ge(s_tab[k], 16)
                if k >= 2:
                    act.wait_ge(s_oh_used, HC * (k - 1))
                copy(tab_hi[:, k % 2, :], tab[:, k % TAB_RING, :]).then_inc(s_hi, 1)

            for k in range(NH):
                hot(k)
                if k % 2 == 1:
                    evacuate_hot(act, copy, 0, k - 1)
            for t in range(NT):
                for n in range(NU):
                    if (t * NU + n) % 2 == 0:
                        evacuate_features(act, copy, 0, t, n)
                evacuate_gram(act, copy, 0, t)
                evacuate_pairs(act, copy, 0, t)
                if t == 0:
                    act.wait_ge(s_wgt, WEIGHTS)
                evacuate_layer1(act, relu, 0, t)
                evacuate_layer2(act, relu, 0, t)
                act.wait_ge(s_y, t + 1)
                copy(y[0:1, t * P:(t + 1) * P], pY[0:1, 0:P]).then_inc(s_yr, 1)

        @block.vector
        def _(dve):
            copy = nc.vector.tensor_copy

            def relu(dst, src, bias):
                return nc.vector.tensor_scalar(dst, src, bias, 0.0, ALU.add, ALU.max)

            nc.vector.memset(xT[:, :, :, NF:SLOTS], 0.0).then_inc(s_pad, 1)
            dve.wait_ge(s_const, 1)
            for k in range(NH):
                dve.wait_ge(s_hi, k + 1)
                nc.vector.tensor_tensor(tab_lo[:, k % 2, :], tab[:, k % TAB_RING, :],
                                        tab_hi[:, k % 2, :].bitcast(fp32), ALU.subtract).then_inc(s_lo, 1)
                dve.wait_ge(s_idb[k], 16)
                for c in range(HC):
                    q = k * HC + c
                    if q >= OH_RING:
                        dve.wait_ge(s_oh_used, q - OH_RING + 1)
                    nc.vector.tensor_scalar(onehot[:, q % OH_RING, :], idb[:, k, :], row_of[:, c:c + 1],
                                            None, ALU.is_equal).then_inc(s_oh, 1)
                if k % 2 == 0 and k:
                    evacuate_hot(dve, copy, 1, k - 1)
            evacuate_hot(dve, copy, 1, NH - 1)
            dve.wait_ge(s_wgt, WEIGHTS)
            nc.vector.tensor_tensor(w1s[:, :], w1d[:, 0, :], w1d[:, 1, :], ALU.add).then_inc(s_w1s, 1)
            for t in range(NT):
                for n in range(NU):
                    if (t * NU + n) % 2 == 1:
                        evacuate_features(dve, copy, 1, t, n)
                evacuate_gram(dve, copy, 1, t)
                evacuate_pairs(dve, copy, 1, t)
                dve.wait_ge(s_z, t + 1)
                if t:
                    dve.wait_ge(l1_full[1], t)
                copy(zT[:, 0:KT - 1, :], pZ[:, 0:(KT - 1) * P].rearrange("p (k c) -> p k c", c=P))
                copy(zT[0:KW[-1], KT - 1, :], pZ[0:KW[-1], (KT - 1) * P:KT * P]).then_inc(s_zT, 1)
                evacuate_layer1(dve, relu, 1, t)
                evacuate_layer2(dve, relu, 1, t)

        @block.tensor
        def _(pe):
            mm, tr = nc.tensor.matmul, nc.tensor.transpose

            def hot(k):
                if k >= 2:
                    pe.wait_ge(a_free[k % 2], k // 2)
                pe.wait_ge(s_lo, k + 1)
                for c in range(HC):
                    pe.wait_ge(s_oh, k * HC + c + 1)
                    for part, tp in enumerate((tab_hi, tab_lo)):
                        last = mm(pA[k % 2][:, :], tp[:, k % 2, c * D:(c + 1) * D],
                                  onehot[:, (k * HC + c) % OH_RING, :],
                                  start=(c + part == 0), stop=(c == HC - 1 and part == 1))
                    last.then_inc(s_oh_used, 1)

            def features(t, n):
                v = t * NU + n
                if v == 0:
                    pe.wait_ge(s_const, 3)
                    pe.wait_ge(s_dn, 16)
                if NH // 2 + v // 2:
                    pe.wait_ge(a_free[v % 2], NH // 2 + v // 2)
                for i, slot in enumerate(USES[n]):
                    if slot == 0:
                        src = dn[:, t, :]
                    else:
                        m = COLD.index(slot - 1)
                        if m % PER_LOOKUP_SEM == 0:
                            cnt = min(PER_LOOKUP_SEM, len(COLD) - m)
                            pe.wait_ge(s_rows[t][m // PER_LOOKUP_SEM], 16 * cnt)
                        src = rows[:, t, m, :]
                    last = tr(pA[v % 2][:, i * P:(i + 1) * P], src, ident[:, :])
                last.then_inc(a_full[v % 2], 1)

            def grams(t):
                if t == 0:
                    pe.wait_ge(s_pad, 1)
                for j in range(2):
                    v = (t + 1) * NU
                    pe.wait_ge(a_free[j], NH // 2 + (v + 1 - j) // 2)
                for j in range(2):
                    if t:
                        pe.wait_ge((l1_free[1], l2_free[0])[j], t)
                    for i in range(GB):
                        for q in range(4):
                            x = xT[:, t, q * NG + j * GB + i, :]
                            last = mm(pG[j][q * 32:(q + 1) * 32, i * (NF - 1):(i + 1) * (NF - 1)],
                                      x, x[:, 0:NF - 1], start=True, stop=True)
                    last.then_inc(g_full[j], 1)

            def pairs_to_free(t):
                for j in range(2):
                    pe.wait_ge(g_free[j], t + 1)
                for n in range(CU):
                    j = n % 2
                    if c_uses(t, j) + n // 2:
                        pe.wait_ge(c_free[j], c_uses(t, j) + n // 2)
                    for a in range(n * PB, min((n + 1) * PB, NF - 1)):
                        last = tr(pC[j][0:NG, (a % PB) * P:(a % PB + 1) * P], gram[:, a, :], ident[:, :])
                    last.then_inc(c_full[j], 1)

            def pairs_to_partitions(t):
                for j in range(2):
                    pe.wait_ge(c_free[j], c_uses(t + 1, j))
                if t:
                    pe.wait_ge(l2_free[1], t)
                for k in range(KT):
                    for q in range(4):
                        last = tr(pZ[0:KW[k], k * P + q * NG:k * P + (q + 1) * NG],
                                  zs[:, q, k * P:k * P + KW[k]], ident[0:NG, 0:NG])
                last.then_inc(s_z, 1)

            def mlp(t):
                if t == 0:
                    pe.wait_ge(s_wgt, WEIGHTS)
                    pe.wait_ge(s_w1s, 1)
                else:
                    pe.wait_ge(s_yr, t)
                pe.wait_ge(s_zT, t + 1)
                for n in range(H1 // P):
                    cols, at = slice(n * P, (n + 1) * P), slice(n % UH * P, (n % UH + 1) * P)
                    mm(pL1[n // UH][:, at], w1s[:, cols], dT[:, t, :], start=True, stop=False)
                    for k in range(KT):
                        last = mm(pL1[n // UH][:, at], w1z[0:KW[k], k, cols], zT[0:KW[k], k, :],
                                  start=False, stop=(k == KT - 1))
                    if n % UH == UH - 1:
                        last.then_inc(l1_full[n // UH], 1)
                for n in range(H2 // P):
                    for k in range(H1 // P):
                        if n == 0 and k % UH == 0:
                            pe.wait_ge(l1_free[k // UH], t + 1)
                        last = mm(pL2[n][:, 0:P], w2[:, k, n * P:(n + 1) * P], h1[:, k, :],
                                  start=(k == 0), stop=(k == H1 // P - 1))
                    last.then_inc(l2_full[n], 1)
                for k in range(H2 // P):
                    pe.wait_ge(l2_free[k], t + 1)
                    last = mm(pY[0:1, 0:P], w3[:, k:k + 1], h2[:, k, :], start=(k == 0), stop=(k == H2 // P - 1))
                last.then_inc(s_y, 1)

            for k in range(NH):
                hot(k)
            for t in range(NT):
                for n in range(NU):
                    features(t, n)
                grams(t)
                pairs_to_free(t)
                pairs_to_partitions(t)
                mlp(t)


_INS = ["r_dense_features", "ids"] + [f"tbl_{i}" for i in range(NS)] + ["W_top1", "b_top1", "W_top2", "b_top2", "W_top3"]


def kernel(**inputs):
    import numpy as np
    import concourse.bacc as bacc
    from concourse.bass_utils import run_bass_kernel_spmd as run

    nc = bacc.Bacc("TRN2", target_bir_lowering=False, num_devices=1)
    arrays, aps = {}, {}
    for name in _INS + ["ids_T"]:
        a = np.ascontiguousarray(inputs["ids"].T if name == "ids_T" else inputs[name])
        arrays["in_" + name] = a
        aps[name] = nc.dram_tensor("in_" + name, a.shape, mybir.dt.from_np(a.dtype), kind="ExternalInput").ap()
    out = nc.dram_tensor("out", (B, 1), mybir.dt.float32, kind="ExternalOutput").ap()
    build(nc, aps["r_dense_features"], aps["ids"], aps["ids_T"], [aps[f"tbl_{i}"] for i in range(NS)],
          aps["W_top1"], aps["b_top1"], aps["W_top2"], aps["b_top2"], aps["W_top3"], out)
    return run(nc, [arrays], core_ids=[0]).results[0]["out"]
```

```python
from contextlib import ExitStack

import concourse.bass as bass
from concourse import mybir

B, D, NS = 512, 128, 26
P = 128
NF = NS + 1
NT = B // P
SLOTS = 32
NPAIR = NF * (NF - 1) // 2
PAIR0 = [a * (NF - 1) - a * (a - 1) // 2 for a in range(NF)]
NM = 4
NBLK = (NF - 1 + NM - 1) // NM
NA = NM * NBLK
BW = [NF - 1 - NM * n for n in range(NBLK - 1)]
B0 = [sum(BW[:n]) for n in range(NBLK - 1)]
KP = sum(BW)
DQ = D // NM
LAST = ((1, NM * (NBLK - 1), 1), (2, NM * (NBLK - 1), 2))
assert KP + DQ == P and sum(x[2] for x in LAST) == 3 and NF == NM * (NBLK - 1) + 3
C_BANK = ((0, 3, 6), (1, 2, 4, 5))
H1, H2 = 512, 256
UH = H1 // P // 2
HOT = (3, 5, 6, 10, 11, 12, 13, 20)
NH = len(HOT)
COLD = tuple(f for f in range(NS) if f not in HOT)
HROWS, HC = 125, 8
NG = P // 4
GB = NG // 2
PB = 4
PER_LOOKUP_SEM = 4

TILE_SLOTS = (0,) + tuple(f + 1 for f in COLD)
USES = [TILE_SLOTS[i:i + PB] for i in range(0, len(TILE_SLOTS), PB)]
NU = len(USES)
NPH = NH // 2
STEPS = NPH * HC
SPLITS = [(0, 1), (1, 1), (2, 2)] + [(q, 4) for q in range(4, STEPS, 4)]
HI_AHEAD = 4
TAB_RING, PART_RING, OH_RING = 2, 8, 4
EARLY = {23 + 2 * n: n for n in range(NU - 1)}
LEAD = (0, 1, 2)
assert NH % 2 == 0 and max(EARLY) < STEPS


def splits_before(q):
    return len([1 for first, _ in SPLITS if first <= q])


def runs(slots):
    out = []
    for i, s in enumerate(slots):
        if out and out[-1][0] + out[-1][1] == s:
            out[-1][1] += 1
        else:
            out.append([s, 1, i])
    return out


def schedule():
    for q in range(STEPS):
        yield "hot", None, q
        if q in EARLY:
            yield "features", 0, EARLY[q]
    for t in range(NT + 1):
        if t == 0:
            front = [("features", 0, NU - 1), ("gram", 0, 0), ("features", 1, 0), ("features", 1, 1), ("gram", 0, 1)]
        elif t < NT:
            front = [("features", t, n) for n in range(2 if t == 1 else 0, NU)] + [("gram", t, 0), ("gram", t, 1)]
        else:
            front = []
        if t > 0:
            back = [(x, t - 1, None) for x in ("pairs", "zT", "layer1", "layer2", "layer3")]
        else:
            back = []
        lead = LEAD[min(t, 2)]
        for i in range(max(len(front), len(back) + lead)):
            yield from front[i:i + 1]
            if i >= lead:
                yield from back[i - lead:i - lead + 1]


def build(nc, dense, ids, idsT, tables, W1, b1, W2, b2, W3, out):
    fp32, fp32r, i32 = mybir.dt.float32, mybir.dt.float32r, mybir.dt.int32
    ALU, ACT = mybir.AluOpType, mybir.ActivationFunctionType

    with ExitStack() as ctx:
        def sb(name, shape, dt=fp32):
            return ctx.enter_context(nc.sbuf_tensor(name, shape, dt))

        def bank(name):
            return ctx.enter_context(nc.psum_tensor(name, [P, 512], fp32))

        def sem(name):
            return ctx.enter_context(nc.semaphore(name))

        ident = sb("ident", [P, P])
        row_of = sb("row_of", [HROWS, HC])
        warm = sb("warm", [HROWS, 1])
        idx = sb("idx", [P, NT, NS], i32)
        idb = sb("idb", [HROWS, NH, B], i32)
        rows = sb("rows", [P, NT, len(COLD), D])
        dn = sb("dn", [P, NT, D])
        tab = sb("tab", [HROWS, TAB_RING, 2, HC * D])
        tab_hi = sb("tab_hi", [HROWS, PART_RING, 2, D], fp32r)
        tab_lo = sb("tab_lo", [HROWS, PART_RING, 2, D], fp32r)
        onehot = sb("onehot", [HROWS, OH_RING, 2, B], fp32r)
        xT = sb("xT", [P, NT, P, SLOTS])
        gram = sb("gram", [P, NA, NG])
        zs = sb("zs", [P, NT, 4, P])
        zT = sb("zT", [P, NM, P])
        w1 = sb("w1", [P, NM, H1])
        w1b = sb("w1b", [P, NM, H1])
        w2 = sb("w2", [P, H1 // P, H2])
        w3 = sb("w3", [P, H2 // P])
        bias1 = sb("bias1", [P, H1 // P])
        bias2 = sb("bias2", [P, H2 // P])
        h1 = sb("h1", [P, H1 // P, P])
        h2 = sb("h2", [P, H2 // P, P])
        y = sb("y", [1, B])

        pA = [bank("pA0"), bank("pA1")]
        pG = [bank("pG0"), bank("pG1")]
        pC = [bank("pC0"), bank("pC1")]
        pZ = [bank("pZ0"), bank("pZ1")]
        pHot = [pG, pC]
        pL1, pL2, pY = pC, pZ, pZ[1]
        s_idx, s_dn, s_wgt = sem("s_idx"), sem("s_dn"), sem("s_wgt")
        s_idb = [sem(f"s_idb{k}") for k in range(NH)]
        s_tab = [sem(f"s_tab{h}") for h in range(NH)]
        NL = (len(COLD) + PER_LOOKUP_SEM - 1) // PER_LOOKUP_SEM
        s_rows = [[sem(f"s_rows{t}_{n}") for n in range(NL)] for t in range(NT)]
        s_const = sem("s_const")
        s_pad = sem("s_pad")
        s_zd = sem("s_zd")
        s_w1s = sem("s_w1s")
        s_hi, s_lo = sem("s_hi"), sem("s_lo")
        s_oh = sem("s_oh")
        s_oh_used = sem("s_oh_used")
        hot_free = sem("hot_free")
        a_full = [sem("a_full0"), sem("a_full1")]
        a_free = [sem("a_free0"), sem("a_free1")]
        g_full = [sem("g_full0"), sem("g_full1")]
        g_free = [sem("g_free0"), sem("g_free1")]
        c_full = [sem("c_full0"), sem("c_full1")]
        c_free = [sem("c_free0"), sem("c_free1")]
        s_first = sem("s_first")
        z_full, z_free = [sem("z_full0"), sem("z_full1")], [sem("z_free0"), sem("z_free1")]
        s_zero = sem("s_zero")
        l1_full, l1_free = [sem("l1_full0"), sem("l1_full1")], [sem("l1_free0"), sem("l1_free1")]
        l2_full, l2_free = [sem("l2_full0"), sem("l2_full1")], [sem("l2_free0"), sem("l2_free1")]
        s_y, s_yr = sem("s_y"), sem("s_yr")
        s_out = sem("s_out")

        def evacuate_features(eng, copy, j, t, n):
            v = t * NU + n
            eng.wait_ge(a_full[j], v // 2 + 1)
            for first, count, at in runs(USES[n]):
                last = copy(xT[:, t, :, first:first + count].rearrange("p c f -> p f c"),
                            pA[j][:, at * P:(at + count) * P].rearrange("p (f c) -> p f c", f=count))
            last.then_inc(a_free[j], 1)

        def split_view(first, count, buf):
            r = first % PART_RING
            return buf[:, r:r + count, :, :].rearrange("p c i d -> p i c d")

        def split_tab(first, count):
            c = first % HC
            return tab[:, first // HC % TAB_RING, :, c * D:(c + count) * D].rearrange("p i (c d) -> p i c d", d=D)

        def evacuate_hot(eng, copy, pair, i):
            eng.wait_ge(s_oh_used, HC * (pair + 1))
            slot = HOT[2 * pair + i] + 1
            copy(xT[:, :, :, slot].rearrange("p t c -> p (t c)"), pHot[pair % 2][i][:, :]).then_inc(hot_free, 1)

        def evacuate_gram(eng, copy, j, t):
            eng.wait_ge(g_full[j], t + 1)
            if t:
                for i in range(2):
                    eng.wait_ge(c_full[i], t)
            copy(gram[:, :, j * GB:(j + 1) * GB],
                 pG[j][:, 0:GB * NA].rearrange("p (g a) -> p a g", g=GB)).then_inc(g_free[j], 1)

        def evacuate_pairs(eng, copy, j, t):
            eng.wait_ge(c_full[j], t + 1)
            for i, n in enumerate(C_BANK[j]):
                src = pC[j][:, i * P:(i + 1) * P].rearrange("p (q b) -> p q b", q=4)
                if n < NBLK - 1:
                    last = copy(zs[:, t, :, B0[n]:B0[n] + BW[n]], src[:, :, NM * n + 1:NF])
                    if n == 0:
                        last.then_inc(s_first, 1)
                else:
                    eng.wait_ge(s_first, t + 1)
                    for m, b0, count in LAST:
                        rng = slice(m * NG, (m + 1) * NG)
                        last = copy(zs[rng, t, :, 0:count], src[rng, :, b0:b0 + count])
            last.then_inc(c_free[j], 1)

        def evacuate_zT(eng, copy, j, t):
            eng.wait_ge(z_full[j], t + 1)
            if t:
                eng.wait_ge(l1_full[1], t)
            copy(zT[:, :, 2 * j * NG:2 * (j + 1) * NG].rearrange("p m (q g) -> p m q g", q=2),
                 pZ[j][:, 0:2 * P].rearrange("p (q m g) -> p m q g", q=2, m=NM)).then_inc(z_free[j], 1)

        def evacuate_layer1(eng, relu, j, t):
            eng.wait_ge(l1_full[j], t + 1)
            if t:
                eng.wait_ge(l2_full[1], t)
            for i in range(UH):
                n = j * UH + i
                last = relu(h1[:, n, :], pL1[j][:, i * P:(i + 1) * P], bias1[:, n:n + 1])
            last.then_inc(l1_free[j], 1)

        def evacuate_layer2(eng, relu, j, t):
            eng.wait_ge(l2_full[j], t + 1)
            if t:
                eng.wait_ge(s_y, t)
            relu(h2[:, j, :], pL2[j][:, 0:P], bias2[:, j:j + 1]).then_inc(l2_free[j], 1)

        block = ctx.enter_context(nc.Block())

        @block.sync
        def _(sp):
            def load_pair(p):
                if p >= TAB_RING:
                    sp.wait_ge(s_lo, splits_before((p - TAB_RING + 1) * HC - 1))
                for half in range(2):
                    for i in range(2):
                        cols = slice(half * HC // 2 * D, (half + 1) * HC // 2 * D)
                        sp.dma_start(tab[:, p % TAB_RING, i, cols],
                                     tables[HOT[2 * p + i]].rearrange("(p c) d -> p (c d)", c=HC)[:, cols]
                                     ).then_inc(s_tab[2 * p + half], 16)

            def load_hot_ids(p):
                for k in (2 * p, 2 * p + 1):
                    sp.dma_start(idb[:, k, :], idsT[HOT[k], :].partition_broadcast(HROWS)).then_inc(s_idb[k], 16)

            sp.dma_start(idx[:, :, :], ids.rearrange("(t c) f -> c t f", t=NT)).then_inc(s_idx, 16)
            load_hot_ids(0)
            load_pair(0)
            load_pair(1)
            load_hot_ids(1)
            load_pair(2)
            load_hot_ids(2)
            load_hot_ids(3)
            sp.dma_start(dn[:, :, :], dense.rearrange("(t c) d -> c t d", t=NT)).then_inc(s_dn, 16)
            load_pair(3)
            for m in range(NM):
                sp.dma_start(zs[m * NG:(m + 1) * NG, :, :, KP:P],
                             dense[:, m * DQ:(m + 1) * DQ].rearrange("(t q g) i -> g t q i", t=NT, q=4)).then_inc(s_zd, 16)
            sp.wait_ge(s_zero, 1)
            for i, dst in enumerate((w1, w1b)):
                r = i * (D + NPAIR)
                sp.dma_start(dst[KP:P, :, :], W1[r:r + D, :].rearrange("(m p) h -> p m h", m=NM)).then_inc(s_wgt, 16)
            for a in range(NM * (NBLK - 1)):
                n, m = divmod(a, NM)
                r, p = D + PAIR0[a], B0[n] + m
                sp.dma_start(w1[p:p + NF - 1 - a, m, :], W1[r:r + NF - 1 - a, :]).then_inc(s_wgt, 16)
            for m, b0, count in LAST:
                for i in range(count):
                    r = D + PAIR0[b0 + i] + NM * (NBLK - 1) + m - (b0 + i) - 1
                    sp.dma_start(w1[i:i + 1, m, :], W1[r:r + 1, :]).then_inc(s_wgt, 16)
            sp.dma_start(w2[:, :, :], W2.rearrange("(n p) m -> p n m", p=P)).then_inc(s_wgt, 16)
            with nc.allow_non_contiguous_dma(reason="three vectors of a few hundred numbers"):
                sp.dma_start(w3[:, :], W3.rearrange("(n p) o -> p (n o)", p=P)).then_inc(s_wgt, 16)
                sp.dma_start(bias1[:, :], b1.rearrange("(n p) -> p n", p=P)).then_inc(s_wgt, 16)
                sp.dma_start(bias2[:, :], b2.rearrange("(n p) -> p n", p=P)).then_inc(s_wgt, 16)
            sp.wait_ge(s_yr, NT)
            sp.dma_start(out.rearrange("(a n) o -> a (n o)", a=1), y[:, :]).then_inc(s_out, 16)
            sp.wait_ge(s_out, 16)

        WEIGHTS = 16 * (2 + NF - 1 - 2 + 3 + 4)

        @block.gpsimd
        def _(pool):
            nc.gpsimd.iota(row_of[:, :], [[1, HC]], base=0, channel_multiplier=HC,
                           allow_small_or_imprecise_dtypes=True).then_inc(s_const, 1)
            nc.gpsimd.memset(ident[:, :], 0.0).then_inc(s_const, 1)
            pool.wait_ge(s_const, 2)
            nc.gpsimd.affine_select(out=ident[:, :], in_=ident[:, :], compare_op=ALU.not_equal, fill=1.0,
                                    base=0, pattern=[[-1, P]], channel_multiplier=1).then_inc(s_const, 1)
            pool.wait_ge(s_idx, 16)
            for t in range(NT):
                for i, f in enumerate(COLD):
                    pool.indirect_dma_start(rows[:, t, i, :], None, tables[f],
                                            bass.IndirectOffsetOnAxis(ap=idx[:, t, f:f + 1], axis=0)
                                            ).then_inc(s_rows[t][i // PER_LOOKUP_SEM], 16)

        @block.scalar
        def _(act):
            copy = nc.scalar.copy

            def relu(dst, src, bias):
                return nc.scalar.activation(dst, src, ACT.Relu, bias=bias)

            def high_parts(first, count):
                act.wait_ge(s_tab[first * 2 // HC], 32)
                if first + count > PART_RING:
                    act.wait_ge(s_oh_used, first + count - PART_RING)
                copy(split_view(first, count, tab_hi), split_tab(first, count)).then_inc(s_hi, 1)

            act.wait_ge(s_const, 1)
            nc.scalar.activation(warm[:, :], row_of[:, 0:1], ACT.Relu)
            for first, count in SPLITS:
                if first < HI_AHEAD:
                    high_parts(first, count)
            for stage, t, n in schedule():
                if stage == "hot":
                    for first, count in SPLITS:
                        if first == n + HI_AHEAD:
                            high_parts(first, count)
                    if n % HC == 2 and n > HC:
                        for i in range(2):
                            evacuate_hot(act, copy, n // HC - 1, i)
                    elif n == STEPS - 1:
                        evacuate_hot(act, copy, NPH - 1, 0)
                elif stage == "features" and (t == 0 or (t * NU + n) % 2 == 0):
                    evacuate_features(act, copy, (t * NU + n) % 2, t, n)
                elif stage == "gram" and n == 0:
                    evacuate_gram(act, copy, 0, t)
                elif stage == "pairs":
                    evacuate_pairs(act, copy, 0, t)
                elif stage == "zT":
                    evacuate_zT(act, copy, 0, t)
                elif stage == "layer1":
                    if t == 0:
                        act.wait_ge(s_wgt, WEIGHTS)
                    evacuate_layer1(act, relu, 0, t)
                elif stage == "layer2":
                    evacuate_layer2(act, relu, 0, t)
                elif stage == "layer3":
                    act.wait_ge(s_y, t + 1)
                    copy(y[0:1, t * P:(t + 1) * P], pY[0:1, 0:P]).then_inc(s_yr, 1)

        @block.vector
        def _(dve):
            copy = nc.vector.tensor_copy

            def relu(dst, src, bias):
                return nc.vector.tensor_scalar(dst, src, bias, 0.0, ALU.add, ALU.max)

            nc.vector.memset(xT[:, :, :, NF:SLOTS], 0.0).then_inc(s_pad, 1)
            nc.vector.memset(w1[:, :, :], 0.0).then_inc(s_zero, 1)
            dve.wait_ge(s_const, 1)

            def low_parts(first, count):
                dve.wait_ge(s_hi, splits_before(first))
                nc.vector.tensor_tensor(split_view(first, count, tab_lo), split_tab(first, count),
                                        split_view(first, count, tab_hi).bitcast(fp32), ALU.subtract).then_inc(s_lo, 1)

            def one_hot(q):
                pair, c = divmod(q, HC)
                if c == 0:
                    for k in (2 * pair, 2 * pair + 1):
                        dve.wait_ge(s_idb[k], 16)
                if q >= OH_RING:
                    dve.wait_ge(s_oh_used, q - OH_RING + 1)
                nc.vector.tensor_scalar(onehot[:, q % OH_RING, :, :], idb[:, 2 * pair:2 * pair + 2, :],
                                        row_of[:, c:c + 1], None, ALU.is_equal).then_inc(s_oh, 1)

            for stage, t, n in schedule():
                if stage == "hot":
                    one_hot(n)
                    for first, count in SPLITS:
                        if first == n:
                            low_parts(first, count)
                    if n == STEPS - 1:
                        evacuate_hot(dve, copy, n // HC, 1)
                elif stage == "gram" and t == 0 and n == 0:
                    dve.wait_ge(s_wgt, WEIGHTS)
                    nc.vector.tensor_tensor(w1[KP:P, :, :], w1[KP:P, :, :], w1b[KP:P, :, :], ALU.add).then_inc(s_w1s, 1)
                elif stage == "features" and t and (t * NU + n) % 2 == 1:
                    evacuate_features(dve, copy, 1, t, n)
                elif stage == "gram" and n == 1:
                    evacuate_gram(dve, copy, 1, t)
                elif stage == "pairs":
                    evacuate_pairs(dve, copy, 1, t)
                elif stage == "zT":
                    evacuate_zT(dve, copy, 1, t)
                elif stage == "layer1":
                    evacuate_layer1(dve, relu, 1, t)
                elif stage == "layer2":
                    evacuate_layer2(dve, relu, 1, t)

        @block.tensor
        def _(pe):
            mm, tr = nc.tensor.matmul, nc.tensor.transpose

            def hot(q):
                pair, c = divmod(q, HC)
                if c == 0 and pair >= 2:
                    pe.wait_ge(hot_free, 2 * (pair - 1))
                pe.wait_ge(s_lo, splits_before(q))
                pe.wait_ge(s_oh, q + 1)
                for i in range(2):
                    for part, tp in enumerate((tab_hi, tab_lo)):
                        last = mm(pHot[pair % 2][i][:, :], tp[:, q % PART_RING, i, :],
                                  onehot[:, q % OH_RING, i, :],
                                  start=(c + part == 0), stop=(c == HC - 1 and part == 1))
                last.then_inc(s_oh_used, 1)

            def features(t, n):
                v = t * NU + n
                if v == 0:
                    pe.wait_ge(s_const, 3)
                    pe.wait_ge(s_dn, 16)
                if v >= 2:
                    pe.wait_ge(a_free[v % 2], v // 2)
                for i, slot in enumerate(USES[n]):
                    if slot == 0:
                        src = dn[:, t, :]
                    else:
                        m = COLD.index(slot - 1)
                        if m % PER_LOOKUP_SEM == 0:
                            cnt = min(PER_LOOKUP_SEM, len(COLD) - m)
                            pe.wait_ge(s_rows[t][m // PER_LOOKUP_SEM], 16 * cnt)
                        src = rows[:, t, m, :]
                    last = tr(pA[v % 2][:, i * P:(i + 1) * P], src, ident[:, :])
                last.then_inc(a_full[v % 2], 1)

            def grams(t, j):
                if t == 0:
                    pe.wait_ge(s_pad, 1)
                    pe.wait_ge(hot_free, NH)
                for i in range(2):
                    pe.wait_ge(a_free[i], ((t + 1) * NU + 1 - i) // 2)
                if t:
                    pe.wait_ge(g_free[j], t)
                for i in range(GB):
                    for q in range(4):
                        x = xT[:, t, q * NG + j * GB + i, :]
                        last = mm(pG[j][q * 32:(q + 1) * 32, i * NA:(i + 1) * NA], x, x[:, 0:NA],
                                  start=True, stop=True)
                last.then_inc(g_full[j], 1)

            def pairs(t):
                for j in range(2):
                    pe.wait_ge(g_free[j], t + 1)
                for j in range(2):
                    if t:
                        pe.wait_ge(l1_free[j], t)
                    for i, n in enumerate(C_BANK[j]):
                        last = tr(pC[j][:, i * P:(i + 1) * P],
                                  gram[:, n * NM:(n + 1) * NM, :].rearrange("p m g -> p (m g)"), ident[:, :])
                    last.then_inc(c_full[j], 1)

            def pairs_to_partitions(t):
                for j in range(2):
                    pe.wait_ge(c_free[j], t + 1)
                if t:
                    pe.wait_ge(s_yr, t)
                else:
                    pe.wait_ge(s_zd, 16 * NM)
                for j in range(2):
                    for i in range(2):
                        last = tr(pZ[j][:, i * P:(i + 1) * P], zs[:, t, 2 * j + i, :], ident[:, :])
                    last.then_inc(z_full[j], 1)

            def layer1(t):
                if t == 0:
                    pe.wait_ge(s_wgt, WEIGHTS)
                    pe.wait_ge(s_w1s, 1)
                for j in range(2):
                    pe.wait_ge(z_free[j], t + 1)
                for n in range(H1 // P):
                    cols, at = slice(n * P, (n + 1) * P), slice(n % UH * P, (n % UH + 1) * P)
                    for m in range(NM):
                        last = mm(pL1[n // UH][:, at], w1[:, m, cols], zT[:, m, :],
                                  start=(m == 0), stop=(m == NM - 1))
                    if n % UH == UH - 1:
                        last.then_inc(l1_full[n // UH], 1)

            def layer2(t):
                for n in range(H2 // P):
                    for k in range(H1 // P):
                        if n == 0 and k % UH == 0:
                            pe.wait_ge(l1_free[k // UH], t + 1)
                        last = mm(pL2[n][:, 0:P], w2[:, k, n * P:(n + 1) * P], h1[:, k, :],
                                  start=(k == 0), stop=(k == H1 // P - 1))
                    last.then_inc(l2_full[n], 1)

            def layer3(t):
                for k in reversed(range(H2 // P)):
                    pe.wait_ge(l2_free[k], t + 1)
                    last = mm(pY[0:1, 0:P], w3[:, k:k + 1], h2[:, k, :],
                              start=(k == H2 // P - 1), stop=(k == 0))
                last.then_inc(s_y, 1)

            for stage, t, n in schedule():
                if stage == "hot":
                    hot(n)
                elif stage == "features":
                    features(t, n)
                elif stage == "gram":
                    grams(t, n)
                elif stage == "pairs":
                    pairs(t)
                elif stage == "zT":
                    pairs_to_partitions(t)
                elif stage == "layer1":
                    layer1(t)
                elif stage == "layer2":
                    layer2(t)
                elif stage == "layer3":
                    layer3(t)


_INS = ["r_dense_features", "ids"] + [f"tbl_{i}" for i in range(NS)] + ["W_top1", "b_top1", "W_top2", "b_top2", "W_top3"]


def kernel(**inputs):
    import numpy as np
    import concourse.bacc as bacc
    from concourse.bass_utils import run_bass_kernel_spmd as run

    nc = bacc.Bacc("TRN2", target_bir_lowering=False, num_devices=1)
    arrays, aps = {}, {}
    for name in _INS + ["ids_T"]:
        a = np.ascontiguousarray(inputs["ids"].T if name == "ids_T" else inputs[name])
        arrays["in_" + name] = a
        aps[name] = nc.dram_tensor("in_" + name, a.shape, mybir.dt.from_np(a.dtype), kind="ExternalInput").ap()
    out = nc.dram_tensor("out", (B, 1), mybir.dt.float32, kind="ExternalOutput").ap()
    build(nc, aps["r_dense_features"], aps["ids"], aps["ids_T"], [aps[f"tbl_{i}"] for i in range(NS)],
          aps["W_top1"], aps["b_top1"], aps["W_top2"], aps["b_top2"], aps["W_top3"], out)
    return run(nc, [arrays], core_ids=[0]).results[0]["out"]
```

```python
from contextlib import ExitStack

import concourse.bass as bass
from concourse import mybir

B, D, NS = 512, 128, 26
P = 128
NF = NS + 1
NT = B // P
WIDE = 32
NPAIR = NF * (NF - 1) // 2
PAIR0 = [a * (NF - 1) - a * (a - 1) // 2 for a in range(NF)]
NM = 4
NBLK = (NF - 1 + NM - 1) // NM
NA = NM * NBLK
BW = [NF - 1 - NM * n for n in range(NBLK - 1)]
B0 = [sum(BW[:n]) for n in range(NBLK - 1)]
KP = sum(BW)
DQ = D // NM
LAST = ((1, NM * (NBLK - 1), 1), (2, NM * (NBLK - 1), 2))
assert KP + DQ == P and sum(x[2] for x in LAST) == 3 and NF == NM * (NBLK - 1) + 3
C_BANK = ((0, 3, 6), (1, 2, 4, 5))
H1, H2 = 512, 256
UH = H1 // P // 2
HOT = (3, 5, 6, 10, 11, 12, 13, 20, 25)
NH = len(HOT)
LATE = 2
COLD = [tuple(f for f in range(NS) if f not in HOT[:NH if t >= LATE else NH - 1]) for t in range(NT)]
HROWS, HC = 125, 8
NG = P // 4
GB = NG // 2
PB = 4

USES = [[tuple(f + 1 for f in cold[i:i + PB]) for i in range(0, len(cold), PB)] for cold in COLD]
NU = len(USES[0])
assert NH % 2 == 1 and all(len(uses) == NU for uses in USES)
NPH = (NH + 1) // 2
STEPS = NPH * HC
SPLITS = [(0, 1), (1, 1), (2, 2)] + [(q, 4) for q in range(4, STEPS, 4)]
OH_AHEAD = 1
HI_AHEAD = 4
TAB_RING, PART_RING, OH_RING = 2, 8, 6
WARM_UP = 10
STAGES = {"F": "features", "G": "gram", "P": "pairs", "Z": "zT", "1": "layer1", "2": "layer2", "3": "layer3",
          "W": "weights"}
BEHIND_STEP = {8: "F0:0", 14: "F1:0", 22: "F2:0 F3:0", 27: "F4:0", 28: "F0:1 F1:1", 35: "F2:1", 37: "G0:0"}
PLAN = ("G1:0 F3:1 F4:1 F0:2",
        "G0:1 W P:0 F1:2 Z:0 1:0 2:0 F2:2 3:0 G1:1 F3:2 F4:2 P:1",
        "G0:2 Z:1 G1:2 1:1 F0:3 2:1 F1:3 F2:3 3:1 P:2 F3:3 F4:3 Z:2",
        "G0:3 1:2 G1:3 2:2 P:3 3:2 Z:3 1:3 2:3 3:3")
assert max(BEHIND_STEP) < STEPS and NU == 5


def tables_of(pair):
    return range(2 * pair, min(2 * pair + 2, NH))


def first_tile(k):
    return LATE if k == NH - 1 else 0


def pieces_of(pair):
    return (0, 1, 4, HC) if pair == 0 else (0, 4, HC)


def splits_before(q):
    return len([1 for first, _ in SPLITS if first <= q])


def runs(slots):
    out = []
    for i, s in enumerate(slots):
        if out and out[-1][0] + out[-1][1] == s:
            out[-1][1] += 1
        else:
            out.append([s, 1, i])
    return out


def stages(words):
    for word in words.split():
        what, _, t = word.partition(":")
        yield STAGES[what[0]], int(t or 0), int(what[1:] or 0)


def schedule():
    for q in range(STEPS):
        yield "hot", None, q
        yield from stages(BEHIND_STEP.get(q, ""))
    for words in PLAN:
        yield from stages(words)


ON_SCALAR = [(t, n) for words in BEHIND_STEP.values() for stage, t, n in stages(words) if stage == "features"]


def build(nc, dense, denseT, ids, idsT, tables, W1, b1, W2, b2, W3, out):
    fp32, fp32r, i32 = mybir.dt.float32, mybir.dt.float32r, mybir.dt.int32
    ALU, ACT = mybir.AluOpType, mybir.ActivationFunctionType

    with ExitStack() as ctx:
        def sb(name, shape, dt=fp32):
            return ctx.enter_context(nc.sbuf_tensor(name, shape, dt))

        def bank(name):
            return ctx.enter_context(nc.psum_tensor(name, [P, 512], fp32))

        def sem(name):
            return ctx.enter_context(nc.semaphore(name))

        ident = sb("ident", [P, P])
        row_of = sb("row_of", [HROWS, HC])
        warm = sb("warm", [HROWS, 1])
        idx = sb("idx", [P, NT, NS], i32)
        idb = sb("idb", [HROWS, NH, B], i32)
        rows = sb("rows", [P, NT, len(COLD[0]), D])
        dT = sb("dT", [D, B])
        tab = sb("tab", [HROWS, TAB_RING, 2, HC * D])
        tab_hi = sb("tab_hi", [HROWS, PART_RING, 2, D], fp32r)
        tab_lo = sb("tab_lo", [HROWS, PART_RING, 2, D], fp32r)
        onehot = sb("onehot", [HROWS, OH_RING, 2, B], fp32r)
        xT = sb("xT", [P, NT, P * NF + WIDE - NF])
        xs = xT[:, :, 0:P * NF].rearrange("p t (c f) -> p t c f", f=NF)
        gram = sb("gram", [P, NA, NG])
        zs = sb("zs", [P, NT, 4, P])
        zT = sb("zT", [P, NM, P])
        w1 = sb("w1", [P, NM, H1])
        w1b = sb("w1b", [P, NM, H1])
        w2 = sb("w2", [P, H1 // P, H2])
        w3 = sb("w3", [P, H2 // P])
        bias1 = sb("bias1", [P, H1 // P])
        bias2 = sb("bias2", [P, H2 // P])
        h1 = sb("h1", [P, H1 // P, P])
        h2 = sb("h2", [P, H2 // P, P])
        y = sb("y", [P, NT])

        pA = [bank("pA0"), bank("pA1")]
        pG = [bank("pG0"), bank("pG1")]
        pC = [bank("pC0"), bank("pC1")]
        pZ = [bank("pZ0"), bank("pZ1")]
        pHot = [(pG, pC)[p % 2] for p in range(NPH - 1)] + [pZ]
        pL1, pL2 = pC, pZ
        pY = pZ[0][:, P:P + 1]
        s_idx, s_dT, s_wgt = sem("s_idx"), sem("s_dT"), sem("s_wgt")
        s_idb = [sem(f"s_idb{k}") for k in range(NH)]
        s_tab = [[sem(f"s_tab{p}_{c}") for c in pieces_of(p)[:-1]] for p in range(NPH)]
        s_rows = [[sem(f"s_rows{t}_{n}") for n in range(NU)] for t in range(NT)]
        s_const = sem("s_const")
        s_pad = sem("s_pad")
        s_slot0 = sem("s_slot0")
        s_zd = sem("s_zd")
        s_w1s = sem("s_w1s")
        s_hi, s_lo = sem("s_hi"), sem("s_lo")
        s_oh = sem("s_oh")
        s_oh_used = sem("s_oh_used")
        hot_free = sem("hot_free")
        a_full = [sem("a_full0"), sem("a_full1")]
        a_free = [sem("a_free0"), sem("a_free1")]
        g_full = [sem("g_full0"), sem("g_full1")]
        g_free = [sem("g_free0"), sem("g_free1")]
        c_full = [sem("c_full0"), sem("c_full1")]
        c_free = [sem("c_free0"), sem("c_free1")]
        s_first = sem("s_first")
        z_full, z_free = [sem("z_full0"), sem("z_full1")], [sem("z_free0"), sem("z_free1")]
        s_zero = sem("s_zero")
        l1_full, l1_free = [sem("l1_full0"), sem("l1_full1")], [sem("l1_free0"), sem("l1_free1")]
        l2_full, l2_free = [sem("l2_full0"), sem("l2_full1")], [sem("l2_free0"), sem("l2_free1")]
        s_y, s_yr = sem("s_y"), sem("s_yr")
        s_out = sem("s_out")

        def evacuate_features(eng, copy, j, t, n):
            v = t * NU + n
            eng.wait_ge(a_full[j], v // 2 + 1)
            for first, count, at in runs(USES[t][n]):
                last = copy(xs[:, t, :, first:first + count].rearrange("p c f -> p f c"),
                            pA[j][:, at * P:(at + count) * P].rearrange("p (f c) -> p f c", f=count))
            last.then_inc(a_free[j], 1)

        def split_view(first, count, buf):
            r = first % PART_RING
            return buf[:, r:r + count, 0:len(tables_of(first // HC)), :].rearrange("p c i d -> p i c d")

        def split_tab(first, count):
            c = first % HC
            n = len(tables_of(first // HC))
            return tab[:, first // HC % TAB_RING, 0:n, c * D:(c + count) * D].rearrange("p i (c d) -> p i c d", d=D)

        def evacuate_hot(eng, copy, pair, i):
            eng.wait_ge(s_oh_used, HC * (pair + 1))
            k = 2 * pair + i
            t0 = first_tile(k)
            copy(xs[:, t0:, :, HOT[k] + 1],
                 pHot[pair][i][:, t0 * P:].rearrange("p (t c) -> p t c", c=P)).then_inc(hot_free, 1)

        def evacuate_gram(eng, copy, j, t):
            eng.wait_ge(g_full[j], t + 1)
            if t:
                for i in range(2):
                    eng.wait_ge(c_full[i], t)
            copy(gram[:, :, j * GB:(j + 1) * GB],
                 pG[j][:, 0:GB * NA].rearrange("p (g a) -> p a g", g=GB)).then_inc(g_free[j], 1)

        def evacuate_pairs(eng, copy, j, t):
            eng.wait_ge(c_full[j], t + 1)
            for i, n in enumerate(C_BANK[j]):
                src = pC[j][:, i * P:(i + 1) * P].rearrange("p (q b) -> p q b", q=4)
                if n < NBLK - 1:
                    last = copy(zs[:, t, :, B0[n]:B0[n] + BW[n]], src[:, :, NM * n + 1:NF])
                    if n == 0:
                        last.then_inc(s_first, 1)
                else:
                    eng.wait_ge(s_first, t + 1)
                    for m, b0, count in LAST:
                        rng = slice(m * NG, (m + 1) * NG)
                        last = copy(zs[rng, t, :, 0:count], src[rng, :, b0:b0 + count])
            last.then_inc(c_free[j], 1)

        def evacuate_zT(eng, copy, j, t):
            eng.wait_ge(z_full[j], t + 1)
            if t:
                eng.wait_ge(l1_full[1], t)
            copy(zT[:, :, 2 * j * NG:2 * (j + 1) * NG].rearrange("p m (q g) -> p m q g", q=2),
                 pZ[j][:, 0:2 * P].rearrange("p (q m g) -> p m q g", q=2, m=NM)).then_inc(z_free[j], 1)

        def evacuate_layer1(eng, relu, j, t):
            eng.wait_ge(l1_full[j], t + 1)
            if t:
                eng.wait_ge(l2_full[1], t)
            for i in range(UH):
                n = j * UH + i
                last = relu(h1[:, n, :], pL1[j][:, i * P:(i + 1) * P], bias1[:, n:n + 1])
            last.then_inc(l1_free[j], 1)

        def evacuate_layer2(eng, relu, j, t):
            eng.wait_ge(l2_full[j], t + 1)
            if t:
                eng.wait_ge(s_y, t)
            relu(h2[:, j, :], pL2[j][:, 0:P], bias2[:, j:j + 1]).then_inc(l2_free[j], 1)

        block = ctx.enter_context(nc.Block())

        @block.sync
        def _(sp):
            def load_pair(p):
                if p >= TAB_RING:
                    sp.wait_ge(s_lo, splits_before((p - TAB_RING + 1) * HC - 1))
                for n, (c, end) in enumerate(zip(pieces_of(p), pieces_of(p)[1:])):
                    for i in range(len(tables_of(p))):
                        cols = slice(c * D, end * D)
                        sp.dma_start(tab[:, p % TAB_RING, i, cols],
                                     tables[HOT[2 * p + i]].rearrange("(p c) d -> p (c d)", c=HC)[:, cols]
                                     ).then_inc(s_tab[p][n], 16)

            def load_hot_ids(p):
                for k in tables_of(p):
                    sp.dma_start(idb[:, k, :], idsT[HOT[k], :].partition_broadcast(HROWS)).then_inc(s_idb[k], 16)

            sp.dma_start(idx[:, :, :], ids.rearrange("(t c) f -> c t f", t=NT)).then_inc(s_idx, 16)
            load_hot_ids(0)
            load_pair(0)
            load_pair(1)
            load_hot_ids(1)
            sp.dma_start(dT[:, :], denseT[:, :]).then_inc(s_dT, 16)
            load_pair(2)
            load_hot_ids(2)
            for p in range(3, NPH):
                load_hot_ids(p)
            for p in range(3, NPH):
                load_pair(p)
            for m in range(NM):
                sp.dma_start(zs[m * NG:(m + 1) * NG, :, :, KP:P],
                             dense[:, m * DQ:(m + 1) * DQ].rearrange("(t q g) i -> g t q i", t=NT, q=4)).then_inc(s_zd, 16)
            sp.wait_ge(s_zero, 1)
            for i, dst in enumerate((w1, w1b)):
                r = i * (D + NPAIR)
                sp.dma_start(dst[KP:P, :, :], W1[r:r + D, :].rearrange("(m p) h -> p m h", m=NM)).then_inc(s_wgt, 16)
            for a in range(NM * (NBLK - 1)):
                n, m = divmod(a, NM)
                r, p = D + PAIR0[a], B0[n] + m
                sp.dma_start(w1[p:p + NF - 1 - a, m, :], W1[r:r + NF - 1 - a, :]).then_inc(s_wgt, 16)
            for m, b0, count in LAST:
                for i in range(count):
                    r = D + PAIR0[b0 + i] + NM * (NBLK - 1) + m - (b0 + i) - 1
                    sp.dma_start(w1[i:i + 1, m, :], W1[r:r + 1, :]).then_inc(s_wgt, 16)
            sp.dma_start(w2[:, :, :], W2.rearrange("(n p) m -> p n m", p=P)).then_inc(s_wgt, 16)
            with nc.allow_non_contiguous_dma(reason="three vectors of a few hundred numbers"):
                sp.dma_start(w3[:, :], W3.rearrange("(n p) o -> p (n o)", p=P)).then_inc(s_wgt, 16)
                sp.dma_start(bias1[:, :], b1.rearrange("(n p) -> p n", p=P)).then_inc(s_wgt, 16)
                sp.dma_start(bias2[:, :], b2.rearrange("(n p) -> p n", p=P)).then_inc(s_wgt, 16)
            for t in range(NT):
                sp.wait_ge(s_yr, t + 1)
                sp.dma_start(out[t * P:(t + 1) * P, :], y[:, t:t + 1]).then_inc(s_out, 16)
            sp.wait_ge(s_out, 16 * NT)

        WEIGHTS = 16 * (2 + NF - 1 - 2 + 3 + 4)

        @block.gpsimd
        def _(pool):
            nc.gpsimd.iota(row_of[:, :], [[1, HC]], base=0, channel_multiplier=HC,
                           allow_small_or_imprecise_dtypes=True).then_inc(s_const, 1)
            nc.gpsimd.memset(ident[:, :], 0.0).then_inc(s_const, 1)
            pool.wait_ge(s_const, 2)
            nc.gpsimd.affine_select(out=ident[:, :], in_=ident[:, :], compare_op=ALU.not_equal, fill=1.0,
                                    base=0, pattern=[[-1, P]], channel_multiplier=1).then_inc(s_const, 1)
            pool.wait_ge(s_idx, 16)
            for t in range(NT):
                for i, f in enumerate(COLD[t]):
                    pool.indirect_dma_start(rows[:, t, i, :], None, tables[f],
                                            bass.IndirectOffsetOnAxis(ap=idx[:, t, f:f + 1], axis=0)
                                            ).then_inc(s_rows[t][i // PB], 16)

        @block.scalar
        def _(act):
            copy = nc.scalar.copy

            def relu(dst, src, bias):
                return nc.scalar.activation(dst, src, ACT.Relu, bias=bias)

            def high_parts(first, count):
                p = first // HC
                n = len([c for c in pieces_of(p)[1:] if c <= first % HC])
                act.wait_ge(s_tab[p][n], 16 * len(tables_of(p)))
                if first + count > PART_RING:
                    act.wait_ge(s_oh_used, first + count - PART_RING)
                copy(split_view(first, count, tab_hi), split_tab(first, count)).then_inc(s_hi, 1)

            act.wait_ge(s_const, 1)
            nc.scalar.activation(warm[:, :], row_of[:, 0:1], ACT.Relu)
            for first, count in SPLITS:
                if first < HI_AHEAD:
                    high_parts(first, count)
            for stage, t, n in schedule():
                if stage == "hot":
                    for first, count in SPLITS:
                        if first == n + HI_AHEAD:
                            high_parts(first, count)
                    if n == HI_AHEAD:
                        act.wait_ge(s_dT, 16)
                        copy(xs[:, :, :, 0], dT[:, :].rearrange("p (t c) -> p t c", t=NT)).then_inc(s_slot0, 1)
                    if n % HC == 2 and n > HC:
                        for i in range(len(tables_of(n // HC - 1))):
                            evacuate_hot(act, copy, n // HC - 1, i)
                    elif n == STEPS - 1:
                        evacuate_hot(act, copy, NPH - 1, 0)
                elif stage == "features" and ((t, n) in ON_SCALAR or (t * NU + n) % 2 == 0):
                    evacuate_features(act, copy, (t * NU + n) % 2, t, n)
                elif stage == "gram" and n == 0:
                    evacuate_gram(act, copy, 0, t)
                elif stage == "pairs":
                    evacuate_pairs(act, copy, 0, t)
                elif stage == "zT":
                    evacuate_zT(act, copy, 0, t)
                elif stage == "layer1":
                    if t == 0:
                        act.wait_ge(s_wgt, WEIGHTS)
                    evacuate_layer1(act, relu, 0, t)
                elif stage == "layer2":
                    evacuate_layer2(act, relu, 0, t)
                elif stage == "layer3":
                    act.wait_ge(s_y, t + 1)
                    copy(y[:, t:t + 1], pY).then_inc(s_yr, 1)

        @block.vector
        def _(dve):
            copy = nc.vector.tensor_copy

            def relu(dst, src, bias):
                return nc.vector.tensor_scalar(dst, src, bias, 0.0, ALU.add, ALU.max)

            nc.vector.memset(xT[:, :, P * NF:], 0.0).then_inc(s_pad, 1)
            nc.vector.memset(w1[:, :, :], 0.0).then_inc(s_zero, 1)
            dve.wait_ge(s_const, 1)

            def low_parts(first, count):
                dve.wait_ge(s_hi, splits_before(first))
                nc.vector.tensor_tensor(split_view(first, count, tab_lo), split_tab(first, count),
                                        split_view(first, count, tab_hi).bitcast(fp32), ALU.subtract).then_inc(s_lo, 1)

            def one_hot(q):
                pair, c = divmod(q, HC)
                if c == 0:
                    for k in tables_of(pair):
                        dve.wait_ge(s_idb[k], 16)
                if q >= OH_RING:
                    dve.wait_ge(s_oh_used, q - OH_RING + 1)
                ks = tables_of(pair)
                c0 = first_tile(ks[0]) * P
                nc.vector.tensor_scalar(onehot[:, q % OH_RING, 0:len(ks), c0:], idb[:, ks[0]:ks[-1] + 1, c0:],
                                        row_of[:, c:c + 1], None, ALU.is_equal).then_inc(s_oh, 1)

            for stage, t, n in schedule():
                if stage == "hot":
                    if n == 0:
                        for q in range(OH_AHEAD):
                            one_hot(q)
                    for first, count in SPLITS:
                        if first == n:
                            low_parts(first, count)
                    if n + OH_AHEAD < STEPS:
                        one_hot(n + OH_AHEAD)
                    if n == STEPS - 1 and len(tables_of(n // HC)) == 2:
                        evacuate_hot(dve, copy, n // HC, 1)
                elif stage == "weights":
                    dve.wait_ge(s_wgt, WEIGHTS)
                    nc.vector.tensor_tensor(w1[KP:P, :, :], w1[KP:P, :, :], w1b[KP:P, :, :], ALU.add).then_inc(s_w1s, 1)
                elif stage == "features" and (t, n) not in ON_SCALAR and (t * NU + n) % 2 == 1:
                    evacuate_features(dve, copy, 1, t, n)
                elif stage == "gram" and n == 1:
                    evacuate_gram(dve, copy, 1, t)
                elif stage == "pairs":
                    evacuate_pairs(dve, copy, 1, t)
                elif stage == "zT":
                    evacuate_zT(dve, copy, 1, t)
                elif stage == "layer1":
                    evacuate_layer1(dve, relu, 1, t)
                elif stage == "layer2":
                    evacuate_layer2(dve, relu, 1, t)

        @block.tensor
        def _(pe):
            mm, tr = nc.tensor.matmul, nc.tensor.transpose

            def hot(q):
                pair, c = divmod(q, HC)
                if c == 0 and 2 <= pair < NPH - 1:
                    pe.wait_ge(hot_free, 2 * (pair - 1))
                pe.wait_ge(s_lo, splits_before(q))
                pe.wait_ge(s_oh, q + 1)
                for i, k in enumerate(tables_of(pair)):
                    c0 = first_tile(k) * P
                    for part, tp in enumerate((tab_hi, tab_lo)):
                        last = mm(pHot[pair][i][:, c0:], tp[:, q % PART_RING, i, :],
                                  onehot[:, q % OH_RING, i, c0:],
                                  start=(c + part == 0), stop=(c == HC - 1 and part == 1))
                last.then_inc(s_oh_used, 1)

            def features(t, n):
                v = t * NU + n
                if v >= 2:
                    pe.wait_ge(a_free[v % 2], v // 2)
                pe.wait_ge(s_rows[t][n], 16 * len(USES[t][n]))
                for i in range(len(USES[t][n])):
                    last = tr(pA[v % 2][:, i * P:(i + 1) * P], rows[:, t, n * PB + i, :], ident[:, :])
                last.then_inc(a_full[v % 2], 1)

            def grams(t, j):
                if t == 0:
                    pe.wait_ge(s_pad, 1)
                    pe.wait_ge(s_slot0, 1)
                    pe.wait_ge(hot_free, NH - 1)
                if t == LATE:
                    pe.wait_ge(hot_free, NH)
                for i in range(2):
                    pe.wait_ge(a_free[i], ((t + 1) * NU + 1 - i) // 2)
                if t:
                    pe.wait_ge(g_free[j], t)
                for i in range(GB):
                    for q in range(4):
                        c = (q * NG + j * GB + i) * NF
                        last = mm(pG[j][q * WIDE:(q + 1) * WIDE, i * NA:(i + 1) * NA],
                                  xT[:, t, c:c + WIDE], xT[:, t, c:c + NA],
                                  start=True, stop=True)
                last.then_inc(g_full[j], 1)

            def pairs(t):
                for j in range(2):
                    pe.wait_ge(g_free[j], t + 1)
                for j in range(2):
                    if t:
                        pe.wait_ge(l1_free[j], t)
                    for i, n in enumerate(C_BANK[j]):
                        last = tr(pC[j][:, i * P:(i + 1) * P],
                                  gram[:, n * NM:(n + 1) * NM, :].rearrange("p m g -> p (m g)"), ident[:, :])
                    last.then_inc(c_full[j], 1)

            def pairs_to_partitions(t):
                for j in range(2):
                    pe.wait_ge(c_free[j], t + 1)
                if t:
                    pe.wait_ge(s_yr, t)
                    pe.wait_ge(l2_free[1], t)
                else:
                    pe.wait_ge(s_zd, 16 * NM)
                    pe.wait_ge(hot_free, NH)
                for j in range(2):
                    for i in range(2):
                        last = tr(pZ[j][:, i * P:(i + 1) * P], zs[:, t, 2 * j + i, :], ident[:, :])
                    last.then_inc(z_full[j], 1)

            def layer1(t):
                if t == 0:
                    pe.wait_ge(s_wgt, WEIGHTS)
                    pe.wait_ge(s_w1s, 1)
                for j in range(2):
                    pe.wait_ge(z_free[j], t + 1)
                for n in range(H1 // P):
                    cols, at = slice(n * P, (n + 1) * P), slice(n % UH * P, (n % UH + 1) * P)
                    for m in range(NM):
                        last = mm(pL1[n // UH][:, at], w1[:, m, cols], zT[:, m, :],
                                  start=(m == 0), stop=(m == NM - 1))
                    if n % UH == UH - 1:
                        last.then_inc(l1_full[n // UH], 1)

            def layer2(t):
                for half in range(2):
                    pe.wait_ge(l1_free[half], t + 1)
                    for n in range(H2 // P):
                        for k in range(half * UH, (half + 1) * UH):
                            last = mm(pL2[n][:, 0:P], w2[:, k, n * P:(n + 1) * P], h1[:, k, :],
                                      start=(k == 0), stop=(k == H1 // P - 1))
                        if half:
                            last.then_inc(l2_full[n], 1)

            def layer3(t):
                for k in range(H2 // P):
                    pe.wait_ge(l2_free[k], t + 1)
                    last = mm(pY, h2[:, k, :], w3[:, k:k + 1], start=(k == 0), stop=(k == H2 // P - 1))
                last.then_inc(s_y, 1)

            pe.wait_ge(s_const, 3)
            for _ in range(WARM_UP):
                mm(pA[0][:, 0:P], ident[:, :], ident[:, :], start=True, stop=True)
            for stage, t, n in schedule():
                if stage == "hot":
                    hot(n)
                elif stage == "features":
                    features(t, n)
                elif stage == "gram":
                    grams(t, n)
                elif stage == "pairs":
                    pairs(t)
                elif stage == "zT":
                    pairs_to_partitions(t)
                elif stage == "layer1":
                    layer1(t)
                elif stage == "layer2":
                    layer2(t)
                elif stage == "layer3":
                    layer3(t)


_INS = ["r_dense_features", "ids"] + [f"tbl_{i}" for i in range(NS)] + ["W_top1", "b_top1", "W_top2", "b_top2", "W_top3"]


_TRANSPOSED = {"ids_T": "ids", "dense_T": "r_dense_features"}


def kernel(**inputs):
    import numpy as np
    import concourse.bacc as bacc
    from concourse.bass_utils import run_bass_kernel_spmd as run

    nc = bacc.Bacc("TRN2", target_bir_lowering=False, num_devices=1)
    arrays, aps = {}, {}
    for name in _INS + list(_TRANSPOSED):
        a = np.ascontiguousarray(inputs[_TRANSPOSED[name]].T if name in _TRANSPOSED else inputs[name])
        arrays["in_" + name] = a
        aps[name] = nc.dram_tensor("in_" + name, a.shape, mybir.dt.from_np(a.dtype), kind="ExternalInput").ap()
    out = nc.dram_tensor("out", (B, 1), mybir.dt.float32, kind="ExternalOutput").ap()
    build(nc, aps["r_dense_features"], aps["dense_T"], aps["ids"], aps["ids_T"], [aps[f"tbl_{i}"] for i in range(NS)],
          aps["W_top1"], aps["b_top1"], aps["W_top2"], aps["b_top2"], aps["W_top3"], out)
    return run(nc, [arrays], core_ids=[0]).results[0]["out"]
```
